# Optimizing a Trainium2 kernel written in Bass

```python
import numpy as np
import jax
import jax.numpy as jnp

def _softmax(x, axis=-1):
    return jax.nn.softmax(x, axis=axis)

def _gelu(x):
    return jax.nn.gelu(x, approximate=True)

def _silu(x):
    return jax.nn.silu(x)

def _sigmoid(x):
    return jax.nn.sigmoid(x)

def _layernorm(x, axis=-1, eps=1e-05):
    m = jnp.mean(x, axis=axis, keepdims=True)
    v = jnp.var(x, axis=axis, keepdims=True)
    return (x - m) / jnp.sqrt(v + eps)

def _scatter_add(tgt, idx, src, axis=0):
    return tgt.at[idx].add(src)

def _segment_sum(src, seg, n):
    return jax.ops.segment_sum(src, seg, n)
kernel_name = 'mk_gps_d1_gnn_r32_a1e355'

def setup_inputs(seed: int=0):
    np.random.seed(seed)
    _w = jnp.asarray

    def _rec_inputs():
        import jax
        import jax.numpy as jnp
        _gk = jax.random.key(seed)
        x = -0.0002117 + 1 * jax.random.normal(jax.random.fold_in(_gk, 1), (3125, 256), jnp.float32)
        src = jax.random.randint(jax.random.fold_in(_gk, 2), (50000,), 0, 3125, jnp.int32)
        dst = jax.random.randint(jax.random.fold_in(_gk, 3), (50000,), 0, 3125, jnp.int32)
        _o = jnp.argsort(dst, stable=True)
        src = src[_o]
        dst = dst[_o]
        edge_weight = jax.random.uniform(jax.random.fold_in(_gk, 12), (50000,), jnp.float32, 0.0, 1)
        return (x, src, dst, edge_weight)
    x, src, dst, edge_weight = _rec_inputs()

    def _L0_gnn_setup():
        import jax, jax.numpy as jnp
        import numpy as np
        N = 3125
        E = 100000
        F_IN = 256
        F_OUT = 256
        key = jax.random.key(seed)
        k1, k2, k3, k4, k5 = jax.random.split(key, 5)
        x = jax.random.normal(k1, (N, F_IN), dtype=jnp.float32)
        edge_row = jax.random.randint(k2, (E,), 0, N, dtype=jnp.int32)
        edge_col = jax.random.randint(k3, (E,), 0, N, dtype=jnp.int32)
        edge_val = jax.random.uniform(k4, (E,), dtype=jnp.float32)
        W = jax.random.normal(k5, (2 * F_IN, F_OUT), dtype=jnp.float32) * (1.0 / np.sqrt(2 * F_IN))
        b = jnp.zeros((F_OUT,), dtype=jnp.float32)
        return {'x': x, 'edge_row': edge_row, 'edge_col': edge_col, 'edge_val': edge_val, 'W': W, 'b': b}
    _L0_gnn_all = _L0_gnn_setup()
    _L0_gnn_in = {k: v for k, v in _L0_gnn_all.items() if k in ('W', 'b')}
    del _L0_gnn_all

    def _L0_mix_setup():
        import jax, jax.numpy as jnp
        import numpy as np
        C_CURV = 1.0
        MIN_NORM = 1e-15
        BALL_EPS = 1e-05
        ATT_EPS = 1e-15
        DIM = 32

        def _norm(x):
            return jnp.clip(jnp.linalg.norm(x, axis=-1, keepdims=True), MIN_NORM)

        def proj(x, c):
            maxnorm = (1.0 - BALL_EPS) / jnp.sqrt(c)
            n = _norm(x)
            return jnp.where(n > maxnorm, x / n * maxnorm, x)

        def expmap0(u, c):
            sc = jnp.sqrt(c)
            n = _norm(u)
            return jnp.tanh(sc * n) * u / (sc * n)

        def logmap0(p, c):
            sc = jnp.sqrt(c)
            n = _norm(p)
            return jnp.arctanh(jnp.clip(sc * n, -1.0 + 1e-07, 1.0 - 1e-07)) * p / (sc * n)

        def mobius_add(x, y, c):
            x2 = jnp.sum(x * x, -1, keepdims=True)
            y2 = jnp.sum(y * y, -1, keepdims=True)
            xy = jnp.sum(x * y, -1, keepdims=True)
            num = (1 + 2 * c * xy + c * y2) * x + (1 - c * x2) * y
            den = 1 + 2 * c * xy + c * c * x2 * y2
            return num / jnp.clip(den, MIN_NORM)

        def conv1d(x, w, pad, groups=1):
            return jax.lax.conv_general_dilated(x, w, (1,), [(pad, pad)], dimension_numbers=('NCH', 'OIH', 'NCH'), feature_group_count=groups)

        def batchnorm(x, gamma, beta):
            mean = jnp.mean(x, axis=(0, 2), keepdims=True)
            var = jnp.var(x, axis=(0, 2), keepdims=True)
            xn = (x - mean) * jax.lax.rsqrt(var + 1e-05)
            return gamma[None, :, None] * xn + beta[None, :, None]

        def _reference_tuple_inner(x, w_qkv, bn_gamma, bn_beta, w_dw, w_pw, w_res, b_res):
            c = C_CURV
            h = logmap0(proj(x, c), c)
            h = jnp.transpose(h, (1, 2, 0))
            h = conv1d(h, w_qkv, pad=2)
            h = batchnorm(h, bn_gamma, bn_beta)
            h = jax.nn.relu(jnp.transpose(h, (2, 0, 1)))
            qkv = proj(expmap0(h, c), c)
            t = jnp.transpose(logmap0(proj(qkv, c), c), (1, 2, 0))
            s = conv1d(t, w_dw, pad=2, groups=t.shape[1])
            s = conv1d(s, w_pw, pad=0, groups=t.shape[1] // DIM)
            cat = jnp.concatenate([t, s], axis=1)
            ai = proj(expmap0(jnp.transpose(cat, (2, 0, 1)), c), c)
            t2 = logmap0(proj(ai, c), c)
            L, N, C2 = t2.shape
            g = C2 // (3 * DIM)
            qkv3 = jnp.transpose(t2, (1, 2, 0)).reshape(N, g, 3 * DIM, L)
            q, k, v = jnp.split(qkv3, 3, axis=2)
            q = jax.nn.relu(q)
            k = jax.nn.relu(k)
            vk = jnp.einsum('ngdl,ngel->ngde', v, k)
            out = jnp.einsum('ngde,ngdl->ngdl', vk, q)
            out = out / (jnp.sum(v, -1, keepdims=True) + ATT_EPS)
            out = jnp.transpose(out.reshape(N, g * DIM, L), (2, 0, 1))
            fx_h = proj(expmap0(out, c), c)
            ft = jnp.transpose(logmap0(proj(fx_h, c), c), (1, 2, 0))
            ft = conv1d(ft, w_res, pad=0) + b_res[None, :, None]
            fx = proj(expmap0(jnp.transpose(ft, (2, 0, 1)), c), c)
            residual = mobius_add(fx, x, c)
            return (fx, residual)
        key = jax.random.key(seed)
        ks = jax.random.split(key, 6)
        L, N, C, TD = (64, 16, 256, 256)
        x = jax.random.normal(ks[0], (L, N, C), jnp.float32) * 0.05
        w_qkv = jax.random.normal(ks[1], (3 * TD, C, 5), jnp.float32) / np.sqrt(C * 5)
        bn_gamma = jnp.ones((3 * TD,), jnp.float32)
        bn_beta = jnp.zeros((3 * TD,), jnp.float32)
        w_dw = jax.random.normal(ks[2], (3 * TD, 1, 5), jnp.float32) / np.sqrt(5.0)
        w_pw = jax.random.normal(ks[3], (3 * TD, DIM, 1), jnp.float32) / np.sqrt(DIM)
        w_res = jax.random.normal(ks[4], (C, 2 * TD, 1), jnp.float32) / np.sqrt(2 * TD)
        b_res = jnp.zeros((C,), jnp.float32)
        return {'x': x, 'w_qkv': w_qkv, 'bn_gamma': bn_gamma, 'bn_beta': bn_beta, 'w_dw': w_dw, 'w_pw': w_pw, 'w_res': w_res, 'b_res': b_res}
    _L0_mix_all = _L0_mix_setup()
    _L0_mix_in = {k: v for k, v in _L0_mix_all.items() if k in ('w_qkv', 'bn_gamma', 'bn_beta', 'w_dw', 'w_pw', 'w_res', 'b_res')}
    del _L0_mix_all

    def _L0_ffn_setup():
        import jax, jax.numpy as jnp
        import numpy as np
        TOP_K = 2
        LN_EPS = 1e-05
        key = jax.random.key(seed)
        ks = jax.random.split(key, 8)
        B, S, D, E, H = (16, 1024, 256, 8, 1024)
        x = jax.random.normal(ks[0], (B, S, D), dtype=jnp.float32)
        Wr = jax.random.normal(ks[1], (D, E), dtype=jnp.float32) * 0.1
        br = jnp.zeros((E,), dtype=jnp.float32)
        ln_g = jnp.ones((E, D), dtype=jnp.float32)
        ln_b = jnp.zeros((E, D), dtype=jnp.float32)
        W1 = jax.random.normal(ks[2], (E, D, H), dtype=jnp.float32) * (1.0 / np.sqrt(D))
        b1 = jnp.zeros((E, H), dtype=jnp.float32)
        W2 = jax.random.normal(ks[3], (E, H, D), dtype=jnp.float32) * (1.0 / np.sqrt(H))
        b2 = jnp.zeros((E, D), dtype=jnp.float32)
        return {'x': x, 'Wr': Wr, 'br': br, 'ln_g': ln_g, 'ln_b': ln_b, 'W1': W1, 'b1': b1, 'W2': W2, 'b2': b2}
    _L0_ffn_all = _L0_ffn_setup()
    _L0_ffn_in = {k: v for k, v in _L0_ffn_all.items() if k in ('Wr', 'br', 'ln_g', 'ln_b', 'W1', 'b1', 'W2', 'b2')}
    del _L0_ffn_all
    return {'x': x, 'src': src, 'dst': dst, 'edge_weight': edge_weight, 'L0_gnn_W': _L0_gnn_in['W'], 'L0_gnn_b': _L0_gnn_in['b'], 'L0_mix_w_qkv': _L0_mix_in['w_qkv'], 'L0_mix_bn_gamma': _L0_mix_in['bn_gamma'], 'L0_mix_bn_beta': _L0_mix_in['bn_beta'], 'L0_mix_w_dw': _L0_mix_in['w_dw'], 'L0_mix_w_pw': _L0_mix_in['w_pw'], 'L0_mix_w_res': _L0_mix_in['w_res'], 'L0_mix_b_res': _L0_mix_in['b_res'], 'L0_ffn_Wr': _L0_ffn_in['Wr'], 'L0_ffn_br': _L0_ffn_in['br'], 'L0_ffn_ln_g': _L0_ffn_in['ln_g'], 'L0_ffn_ln_b': _L0_ffn_in['ln_b'], 'L0_ffn_W1': _L0_ffn_in['W1'], 'L0_ffn_b1': _L0_ffn_in['b1'], 'L0_ffn_W2': _L0_ffn_in['W2'], 'L0_ffn_b2': _L0_ffn_in['b2']}

def reference(x, src, dst, edge_weight, L0_gnn_W, L0_gnn_b, L0_mix_w_qkv, L0_mix_bn_gamma, L0_mix_bn_beta, L0_mix_w_dw, L0_mix_w_pw, L0_mix_w_res, L0_mix_b_res, L0_ffn_Wr, L0_ffn_br, L0_ffn_ln_g, L0_ffn_ln_b, L0_ffn_W1, L0_ffn_b1, L0_ffn_W2, L0_ffn_b2):
    import jax
    import jax.numpy as jnp

    def _L0_gnn_ref(x, edge_row, edge_col, edge_val, W, b):
        import jax, jax.numpy as jnp
        import numpy as np
        N = 3125
        E = 100000
        F_IN = 256
        F_OUT = 256
        gathered = edge_val[:, None] * x[edge_col]
        support = jax.ops.segment_sum(gathered, edge_row, num_segments=N)
        h = jnp.concatenate([x, support], axis=1)
        out = h @ W + b
        return jax.nn.relu(out)

    def _L0_mix_ref(x, w_qkv, bn_gamma, bn_beta, w_dw, w_pw, w_res, b_res):
        import jax, jax.numpy as jnp
        import numpy as np
        C_CURV = 1.0
        MIN_NORM = 1e-15
        BALL_EPS = 1e-05
        ATT_EPS = 1e-15
        DIM = 32

        def _norm(x):
            return jnp.clip(jnp.linalg.norm(x, axis=-1, keepdims=True), MIN_NORM)

        def proj(x, c):
            maxnorm = (1.0 - BALL_EPS) / jnp.sqrt(c)
            n = _norm(x)
            return jnp.where(n > maxnorm, x / n * maxnorm, x)

        def expmap0(u, c):
            sc = jnp.sqrt(c)
            n = _norm(u)
            return jnp.tanh(sc * n) * u / (sc * n)

        def logmap0(p, c):
            sc = jnp.sqrt(c)
            n = _norm(p)
            return jnp.arctanh(jnp.clip(sc * n, -1.0 + 1e-07, 1.0 - 1e-07)) * p / (sc * n)

        def mobius_add(x, y, c):
            x2 = jnp.sum(x * x, -1, keepdims=True)
            y2 = jnp.sum(y * y, -1, keepdims=True)
            xy = jnp.sum(x * y, -1, keepdims=True)
            num = (1 + 2 * c * xy + c * y2) * x + (1 - c * x2) * y
            den = 1 + 2 * c * xy + c * c * x2 * y2
            return num / jnp.clip(den, MIN_NORM)

        def conv1d(x, w, pad, groups=1):
            return jax.lax.conv_general_dilated(x, w, (1,), [(pad, pad)], dimension_numbers=('NCH', 'OIH', 'NCH'), feature_group_count=groups)

        def batchnorm(x, gamma, beta):
            mean = jnp.mean(x, axis=(0, 2), keepdims=True)
            var = jnp.var(x, axis=(0, 2), keepdims=True)
            xn = (x - mean) * jax.lax.rsqrt(var + 1e-05)
            return gamma[None, :, None] * xn + beta[None, :, None]

        def _reference_tuple_inner(x, w_qkv, bn_gamma, bn_beta, w_dw, w_pw, w_res, b_res):
            c = C_CURV
            h = logmap0(proj(x, c), c)
            h = jnp.transpose(h, (1, 2, 0))
            h = conv1d(h, w_qkv, pad=2)
            h = batchnorm(h, bn_gamma, bn_beta)
            h = jax.nn.relu(jnp.transpose(h, (2, 0, 1)))
            qkv = proj(expmap0(h, c), c)
            t = jnp.transpose(logmap0(proj(qkv, c), c), (1, 2, 0))
            s = conv1d(t, w_dw, pad=2, groups=t.shape[1])
            s = conv1d(s, w_pw, pad=0, groups=t.shape[1] // DIM)
            cat = jnp.concatenate([t, s], axis=1)
            ai = proj(expmap0(jnp.transpose(cat, (2, 0, 1)), c), c)
            t2 = logmap0(proj(ai, c), c)
            L, N, C2 = t2.shape
            g = C2 // (3 * DIM)
            qkv3 = jnp.transpose(t2, (1, 2, 0)).reshape(N, g, 3 * DIM, L)
            q, k, v = jnp.split(qkv3, 3, axis=2)
            q = jax.nn.relu(q)
            k = jax.nn.relu(k)
            vk = jnp.einsum('ngdl,ngel->ngde', v, k)
            out = jnp.einsum('ngde,ngdl->ngdl', vk, q)
            out = out / (jnp.sum(v, -1, keepdims=True) + ATT_EPS)
            out = jnp.transpose(out.reshape(N, g * DIM, L), (2, 0, 1))
            fx_h = proj(expmap0(out, c), c)
            ft = jnp.transpose(logmap0(proj(fx_h, c), c), (1, 2, 0))
            ft = conv1d(ft, w_res, pad=0) + b_res[None, :, None]
            fx = proj(expmap0(jnp.transpose(ft, (2, 0, 1)), c), c)
            residual = mobius_add(fx, x, c)
            return (fx, residual)
        return _reference_tuple_inner(x, w_qkv, bn_gamma, bn_beta, w_dw, w_pw, w_res, b_res)[0]

    def _L0_ffn_ref(x, Wr, br, ln_g, ln_b, W1, b1, W2, b2):
        import jax, jax.numpy as jnp
        import numpy as np
        TOP_K = 2
        LN_EPS = 1e-05
        B, S, D = x.shape
        N = B * S
        xt = x.reshape(N, D)
        logits = xt @ Wr + br
        probs = jax.nn.softmax(logits, axis=-1)
        top_p, top_idx = jax.lax.top_k(probs, TOP_K)
        weights = top_p / top_p.sum(axis=-1, keepdims=True)
        mu = xt.mean(axis=-1, keepdims=True)
        var = ((xt - mu) ** 2).mean(axis=-1, keepdims=True)
        xn = (xt - mu) * jax.lax.rsqrt(var + LN_EPS)
        xe = xn[None, :, :] * ln_g[:, None, :] + ln_b[:, None, :]
        h = jax.nn.gelu(jnp.einsum('end,edh->enh', xe, W1) + b1[:, None, :], approximate=False)
        y = jnp.einsum('enh,ehd->end', h, W2) + b2[:, None, :]
        y_tok = jnp.transpose(y, (1, 0, 2))
        sel = jnp.take_along_axis(y_tok, top_idx[:, :, None], axis=1)
        out = (weights[:, :, None] * sel).sum(axis=1)
        return out.reshape(B, S, D)
    xn = _layernorm(x, axis=-1)
    x = x + _L0_gnn_ref(xn, src, dst, edge_weight, L0_gnn_W, L0_gnn_b) + _L0_mix_ref(xn[None], L0_mix_w_qkv, L0_mix_bn_gamma, L0_mix_bn_beta, L0_mix_w_dw, L0_mix_w_pw, L0_mix_w_res, L0_mix_b_res)[0]
    x = x + _L0_ffn_ref(_layernorm(x, axis=-1)[None], L0_ffn_Wr, L0_ffn_br, L0_ffn_ln_g, L0_ffn_ln_b, L0_ffn_W1, L0_ffn_b1, L0_ffn_W2, L0_ffn_b2)[0]
    return x

_drawn_inputs = setup_inputs


def setup_inputs(seed=0):
    import zlib

    import numpy as np

    out = dict(_drawn_inputs(seed))
    spreads = {'L0_gnn_b': (0.0, 0.1),
     'L0_mix_bn_gamma': (1.0, 0.6),
     'L0_mix_bn_beta': (0.0, 1.265),
     'L0_mix_b_res': (0.0, 0.292),
     'L0_ffn_br': (0.0, 0.1),
     'L0_ffn_ln_g': (1.0, 0.2),
     'L0_ffn_ln_b': (0.0, 0.1),
     'L0_ffn_b1': (0.0, 0.1),
     'L0_ffn_b2': (0.0, 0.1)}
    factors = {'L0_mix_w_dw': 4.081, 'L0_mix_w_pw': 3.925}
    for name, (base, spread) in spreads.items():
        noise = np.random.default_rng([zlib.crc32(name.encode()), seed]).standard_normal(out[name].shape)
        drawn = base * np.exp(spread * noise) if base else spread * noise
        out[name] = jnp.asarray(drawn.astype(out[name].dtype))
    for name, factor in factors.items():
        out[name] = (out[name] * factor).astype(out[name].dtype)
    return out
```

```python
from contextlib import ExitStack

import numpy as np

import concourse.bass as bass
from concourse import mybir

ALU = mybir.AluOpType
ACT = mybir.ActivationFunctionType
AX = mybir.AxisListType.X
F32 = mybir.dt.float32
BF16 = mybir.dt.bfloat16
I32 = mybir.dt.int32
ds = bass.ds

N, C, E = 3125, 256, 50000
T = 125
NT = N // T
EC = E // T
EB = 416
assert EB >= (E + NT * 127) // 128
Q3 = 768
OC = Q3 // 128
NG = 16
TC = 500
NE, H = 8, 1024
TB = (2 * N + NE * 127) // 128
ROUND = 12582912.0
CEIL = 127.0 / 128 - 0.5 + 1.0 / 256
FLOOR = -0.5 + 1.0 / 256
LN_EPS = 1e-5
MAXNORM = float(np.float32(1.0 - 1e-5))
REACH = float(np.arctanh(np.float64(MAXNORM)))
MIN_NORM = 1e-15
ATT_EPS = 1e-15
GR = 16


def need(eng, sem, count):
    if isinstance(count, int) and count <= 0:
        return
    eng.wait_ge(sem, count)


def over(eng, count, ring, body, ahead=0, peel=1):
    last = (count - ahead) // ring
    for t in range(min(peel * ring, count)):
        body(t, t % ring, t // ring)
    if last > peel:
        with eng.Fori(peel, last) as i:
            for s in range(ring):
                body(i * ring + s, s, i)
    for t in range(max(peel, last) * ring, count):
        body(t, t % ring, t // ring)


def build(nc, io):
    with ExitStack() as ctx:
        def sb(name, shape, dt=F32):
            return ctx.enter_context(nc.sbuf_tensor(name, shape, dt))

        def sem(name):
            return ctx.enter_context(nc.semaphore(name))

        A = sb("arena_a", [128, OC * N])
        CC = sb("arena_c", [128, 4 * N + GR * C])
        D = sb("arena_d", [128, 4 * H])
        ED = sb("arena_e", [128, 4 * H])
        X = sb("x", [128, NT, C])
        node = sb("node", [128, 4 * C])
        junk = [node[0:T, 512 * s:512 * s + 512] for s in range(2)]
        small = sb("small", [128, 1600])

        rank = A[0:T, 0:NT * EC].rearrange("p (t c) -> p t c", t=NT)
        member = A[0:T, NT * EC:NT * EC + NT * EC // 2].bitcast(BF16).rearrange("p (t c) -> p t c", t=NT)
        HC = A[:, :].rearrange("p (j n) -> p j n", j=OC)
        W1 = A[:, 0:NE * 2 * H].rearrange("p (e k h) -> p e k h", e=NE, k=2)
        b2s = A[0:3, NE * 2 * H:NE * 2 * H + NE * C // 2].bitcast(BF16).rearrange("p (e c) -> p e c", e=NE)
        XNT = CC[:, 0:2 * N].rearrange("p (k n) -> p k n", k=2)
        S = CC[:, 2 * N:4 * N]
        HT = S.rearrange("p (k n) -> p k n", k=2)
        SUP = HT
        R = CC[:, 4 * N:]
        ring = R.rearrange("p (g c) -> p g c", g=GR)
        W2 = CC[:, 0:NE * 8 * C].rearrange("p (e k c) -> p e k c", e=NE, k=8)

        def cutter(area):
            at = [0]

            def cut(n, dt=F32):
                a = area[:, at[0]:at[0] + n]
                at[0] += n
                return a if dt == F32 else a.bitcast(dt)
            return cut

        cut = cutter(small)
        iota, ident, tri, ones = [cut(128) for _ in range(4)]
        pcol = cut(1)
        jcol = cut(4)
        bg = cut(C)
        Wr = cut(2 * NE).rearrange("p (k e) -> p k e", k=2)
        br = cut(NE)
        lng = cut(2 * NE).rearrange("p (k e) -> p k e", k=2)
        lnb = cut(2 * NE).rearrange("p (k e) -> p k e", k=2)
        gcol = cut(2)
        bcol = cut(2)
        b1T = cut(8 * NE).rearrange("p (j e) -> p j e", j=8)
        b1c = [cut(8) for _ in range(2)]
        ones3 = cut(64, BF16)
        (rstd, s1, nrm, sq_h, sq_s, cc_, epsc, o2, f2, tmpa, tmpb, tmpc, rstd2, wgt1,
         wgt2) = [cut(NT)[0:T, :] for _ in range(15)]
        stats = cut(NT * 6)[0:T, :].rearrange("p (t k) -> p t k", t=NT)
        mv = cut(NT * 2)[0:T, :].rearrange("p (t k) -> p t k", t=NT)
        mean_, var_ = mv[:, :, 0], mv[:, :, 1]

        cut = cutter(ED)
        rec = cut(EC * 4).rearrange("p (c f) -> p c f", f=4)
        slot_i = cut(EC, I32)
        recs = cut(EB * 4).rearrange("p (b f) -> p b f", f=4)
        tile_row = cut(EB // 4, I32)
        stage_i = sb("stage_i", [128, 2, 8], I32)
        stage_r = sb("stage_r", [128, 2, 8, 4])
        gix = sb("gix", [128, 2, 8], I32)
        zero = S[:, 0:1792]
        cut = cutter(S[:, 1792:])
        src_f, tile_f, w_e, e1, e2 = [cut(EC)[0:T, :] for _ in range(5)]
        src_i, dst_i = [cut(EC, I32)[0:T, :] for _ in range(2)]
        ecnt, epre, etot, ebcum, eadj, eblk = [cut(NT)[0:T, :] for _ in range(6)]
        ecmp = cut(4 * NT)[0:EB // 4, :].rearrange("p (q t) -> p q t", q=4)
        etile = cut(4)[0:EB // 4, :]
        epack = cut(1)[0:EB // 4, :]
        etile_i = cut(1, I32)[0:EB // 4, :]

        cut = cutter(D)
        wq = cut(2 * Q3).rearrange("p (k c) -> p k c", k=2)
        bd = cut(OC * 128).rearrange("p (j c) -> p j c", j=OC)
        wres = cut(4 * C).rearrange("p (k c) -> p k c", k=4)
        bres = cut(C)[0:T, :]
        cut = cutter(sb("bn", [128, 50 * OC]))
        dw, gamma, beta, bna, bnb, bnt = [cut(OC) for _ in range(6)]
        bst = cut(42 * OC).rearrange("p (j i k) -> p j i k", j=OC, i=7)
        bmv = cut(2 * OC).rearrange("p (j k) -> p j k", j=OC)
        cut = cutter(R)
        hst = [cut(750).rearrange("p (j n) -> p j n", j=OC) for _ in range(2)]
        xnb = [cut(C)[0:T, :] for _ in range(2)]
        hb = [cut(C)[0:T, :] for _ in range(2)]
        oT = [cut(500).rearrange("p (k n) -> p k n", k=4) for _ in range(2)]
        cut = cutter(S)
        ab = [cut(2 * Q3)[0:T, :] for _ in range(2)]
        den, rden, vr, o0, o1 = [cut(512)[0:T, :] for _ in range(5)]
        ksum = cut(NG)[0:T, :]
        o = [o0, o1]
        b2f = A[0:NE, NE * (2 * H + C // 2):NE * (2 * H + C // 2) + C]
        cut = cutter(D)
        bhi, bmid, blo = [cut(C // 2, BF16)[0:NE, :] for _ in range(3)]
        gnnW = cut(4 * C).rearrange("p (k c) -> p k c", k=4)
        zT = [cut(2 * T).rearrange("p (k n) -> p k n", k=2) for _ in range(2)]
        sel = [cut(T) for _ in range(4)]
        cut = cutter(D)
        gel = [cut(H) for _ in range(2)]
        W1b = [a.rearrange("p (k h) -> p k h", k=2) for a in (D[:, 2 * H:4 * H], ED[:, 0:2 * H])]
        xsb = [node[:, C * s:C * s + C] for s in range(4)]
        xb = [a[0:T, :] for a in xsb]
        cut = cutter(R)
        gst = [cut(2 * T).rearrange("p (k n) -> p k n", k=2) for _ in range(4)]
        cut = cutter(A[:, NE * (2 * H + C // 2):])
        xeT = [cut(2 * 128).rearrange("p (k n) -> p k n", k=2) for _ in range(2)]
        ysb = [cut(C) for _ in range(2)]
        cut = cutter(ED)
        lg, oh1, oh2, cand, t1, t2 = [cut(200)[0:T, :].rearrange("p (t e) -> p t e", t=NT) for _ in range(6)]
        msum, tot, cs, pos = [cut(200)[0:T, :] for _ in range(4)]
        m1, m2, i1, i2, e21, den1 = [cut(NT)[0:T, :] for _ in range(6)]
        sl = cut(2 * NT)[0:T, :].rearrange("p (t c) -> p t c", t=NT)
        bexp, bend, adj8 = [cut(NE)[0:T, :] for _ in range(3)]
        bcmp = cut(TB * NE)[0:1, :].rearrange("p (b e) -> p b e", b=TB)
        brow = cut(TB)[0:1, :]
        slots = sb("slots", [128, NT, 2], I32)
        tix = sb("tix", [128, 4, 2], I32)
        expert_row = sb("expert_row", [128, TB], I32)

        ps = ctx.enter_context(nc.psum_tensor("ps", [128, 8, 512], F32))
        psf = ps[:, :, :].rearrange("p b n -> p (b n)")

        ld_edges, ld_x, ld_w, ld_bd = sem("ld_edges"), sem("ld_x"), sem("ld_w"), sem("ld_bd")
        zeroed = sem("zeroed")
        filled = sem("filled")
        pool_c = sem("pool_c")
        dve_step = sem("dve_step")
        row_in = sem("row_in")
        row_out = sem("row_out")
        act_go = sem("act_go")
        st_done, mix_added, m_gb = sem("stats_done"), sem("mixing_added"), sem("m_gb")
        gnn_in = sem("gnn_in")
        mixed = sem("mixed")
        ft_ready, f2_ready = sem("ft_ready"), sem("f2_ready")
        e_cnt, e_pre = sem("edge_counts"), sem("edge_prefixes")
        slots_ready, rec_ready = sem("slots_ready"), sem("rec_ready")
        etile_ready, tile_row_in = sem("etile_ready"), sem("tile_row_in")
        sc = [sem(f"edge_scattered{k}") for k in range(16)]
        staged, go = sem("edge_staged"), sem("pool_go")
        xn_ready, xn_store = sem("xn_ready"), [sem(f"xn_stored{k}") for k in range(2)]
        h_ready, tp_done, tp_evac = sem("h_ready"), sem("tp_done"), sem("tp_evac")
        qk_mm, qk_act, qk_dve = sem("qk_mm"), sem("qk_act"), sem("qk_dve")
        bn_ready, hc_ready, bd_ready = sem("bn_ready"), sem("hc_ready"), sem("bd_ready")
        p1_st, p1_mm, p1_sq = sem("p1_staged"), sem("p1_mm"), sem("p1_squared")
        p2_st, p2_mm, p2_ab, p2_v = sem("p2_staged"), sem("p2_mm"), sem("p2_ab"), sem("p2_v")
        p2_tr, p2_oT, p2_sq, p2_ft, p2_out = (sem("p2_tr"), sem("p2_oT"), sem("p2_sq"), sem("p2_ft"), sem("p2_out"))
        recs_in = sem("recs_in")
        gix_ready = sem("gix_ready")
        gth = [sem(f"gathered{k}") for k in range(GR)]
        selm, g_mm, g_acc = sem("selection_ready"), sem("g_mm"), sem("g_acc")
        n_st, n_mm, n_v = sem("node_staged"), sem("node_mm"), sem("node_v")
        z_ready, z_tr, z_T, z_lg = sem("z_ready"), sem("z_tr"), sem("z_T"), sem("z_lg")
        routed, prefixed = sem("routed"), sem("prefixed")
        tok_slots = sem("token_slots_ready")
        t_st = sem("token_staged")
        ts = [sem(f"token_scattered{k}") for k in range(8)]
        w1_in, w2_in, b_in, b_split, b3_in = sem("w1_in"), sem("w2_in"), sem("b_in"), sem("b_split"), sem("b3_in")
        xs_in = [sem(f"xs_in{k}") for k in range(4)]
        m_xt, m_xe, m_g1, m_ge, m_g2, m_y = [sem("m_" + n) for n in ("xt", "xe", "g1", "ge", "g2", "y")]
        m_w1, dve_go = sem("m_w1"), sem("dve_go")
        ys_out = [sem(f"ys_stored{k}") for k in range(2)]
        ys_all = sem("ys_all")
        c_ix = sem("combine_index")
        cg = [sem(f"combine_gathered{k}") for k in range(8)]
        c_v = sem("combined")
        out_st = [sem(f"out_stored{k}") for k in range(4)]

        block = ctx.enter_context(nc.Block())

        @block.sync
        def _(sp):
            sp.dma_start(src_i, io["src"].rearrange("(p c) -> p c", p=T)).then_inc(ld_edges, 16)
            sp.dma_start(dst_i, io["dst"].rearrange("(p c) -> p c", p=T)).then_inc(ld_edges, 16)
            sp.dma_start(w_e, io["edge_weight"].rearrange("(p c) -> p c", p=T)).then_inc(ld_edges, 16)
            sp.dma_start(X[0:T, :, :], io["x"].rearrange("(t p) c -> p t c", p=T)).then_inc(ld_x, 16)
            sp.dma_start(wq, io["w_qT"].rearrange("(k p) c -> p k c", p=128)).then_inc(ld_w, 16)
            sp.dma_start(dw, io["w_dw"]).then_inc(ld_w, 16)
            sp.dma_start(gamma, io["bn_gamma"]).then_inc(ld_w, 16)
            sp.dma_start(beta, io["bn_beta"]).then_inc(ld_w, 16)
            sp.dma_start(wres, io["w_resT"].rearrange("(k p) c -> p k c", p=128)).then_inc(ld_w, 16)
            sp.dma_start(bres, io["b_res"].partition_broadcast(T)).then_inc(ld_w, 16)
            sp.dma_start(bg[0:T, :], io["gnn_b"].partition_broadcast(T)).then_inc(ld_w, 16)
            sp.dma_start(Wr, io["Wr"].rearrange("(k p) e -> p k e", p=128)).then_inc(ld_w, 16)
            sp.dma_start(br[0:T, :], io["br"].partition_broadcast(T)).then_inc(ld_w, 16)
            sp.dma_start(b1T, io["b1T"]).then_inc(ld_w, 16)
            sp.dma_start(lng, io["ln_gT"].rearrange("(k p) e -> p k e", p=128)).then_inc(ld_w, 16)
            sp.dma_start(lnb, io["ln_bT"].rearrange("(k p) e -> p k e", p=128)).then_inc(ld_w, 16)
            sp.wait_ge(zeroed, 2)
            for a in range(4):
                sp.dma_start(bd[32 * a:32 * a + 32, :, 32 * a:32 * a + 32],
                             io["w_pwT"].rearrange("k (j a c) -> k j a c", j=OC, a=4)[:, :, a, :]).then_inc(ld_bd, 16)
            sp.dma_start(io["rec_d"].rearrange("(p j) f -> p (j f)", p=128), zero[:, 0:EB * 4]).then_inc(filled, 16)
            per = TB * C // 8
            xs_fill = io["xs_d"].rearrange("(p j) f -> p (j f)", p=128)
            for k in range(8):
                sp.dma_start(xs_fill[:, k * per:(k + 1) * per], zero[:, 0:per]).then_inc(filled, 16)
            sp.wait_ge(etile_ready, 1)
            sp.dma_start(tile_row[0:1, :], etile_i).then_inc(tile_row_in, 16)
            xn_t = io["xn_d"].rearrange("(t p) c -> p t c", p=T)

            def store_xn(t, s, r):
                need(sp, xn_ready, t + 1)
                sp.dma_start(xn_t[:, ds(t, 1), :], xnb[s].unsqueeze(1)).then_inc(xn_store[s], 16)
            over(sp, NT, 2, store_xn)
            for k in range(16):
                sp.wait_ge(sc[k], 16 * (EC // 16))
            sp.dma_start(recs, io["rec_d"].rearrange("(p j) f -> p j f", p=128)).then_inc(recs_in, 16)
            sp.wait_ge(mixed, 1)
            sp.dma_start(gnnW, io["gnn_W"].rearrange("(k p) c -> p k c", p=128)).then_inc(gnn_in, 16)
            for e in range(NE):
                sp.dma_start(W1[:, e, :, :], io["W1"][e].rearrange("(k p) h -> p k h", p=128)).then_inc(w1_in, 16)
            sp.dma_start(b2f, io["b2"]).then_inc(b_in, 16)
            sp.wait_ge(b_split, 1)
            for i, part in enumerate((bhi, bmid, blo)):
                sp.dma_start(b2s[i:i + 1, :, :], part).then_inc(b3_in, 16)
            sp.wait_ge(n_mm, NT)
            for e in range(NE):
                sp.dma_start(W2[:, e, :, :], io["W2"][e].rearrange("(k p) c -> p k c", p=128)).then_inc(w2_in, 16)
            for k in range(8):
                sp.wait_ge(ts[k], 16 * len(range(k // 2, NT, 4)))
            xs_b = io["xs_d"].rearrange("(b p) c -> p b c", p=128)
            ys_b = io["ys_d"].rearrange("(b p) c -> p b c", p=128)
            for b in range(3):
                sp.dma_start(xsb[b], xs_b[:, b, :]).then_inc(xs_in[b], 16)

            def experts_io(b, s, r):
                if not isinstance(b, int) or b + 3 < TB:
                    need(sp, m_xt, b)
                    sp.dma_start(xsb[(s + 3) % 4].unsqueeze(1), xs_b[:, ds(b + 3, 1), :]).then_inc(xs_in[(s + 3) % 4], 16)
                need(sp, m_y, b + 1)
                sp.dma_start(ys_b[:, ds(b, 1), :], ysb[s % 2].unsqueeze(1)).then_inc(ys_out[s % 2], 16)
            over(sp, TB, 4, experts_io, ahead=3)
            for k in range(2):
                sp.wait_ge(ys_out[k], 16 * (TB // 2))
            sp.sem_inc(ys_all, 1)
            out_t = io["out"].rearrange("(t p) c -> p t c", p=T)

            def store_out(t, s, r):
                need(sp, c_v, 2 * (t + 1))
                sp.dma_start(out_t[:, ds(t, 1), :], xb[s].unsqueeze(1)).then_inc(out_st[s], 16)
            over(sp, NT, 4, store_out)
            for s in range(4):
                sp.wait_ge(out_st[s], 16 * len(range(s, NT, 4)))

        @block.gpsimd
        def _(pool):
            nc.gpsimd.iota(iota, [[1, 128]], base=0, channel_multiplier=0,
                           allow_small_or_imprecise_dtypes=True).then_inc(pool_c, 1)
            nc.gpsimd.iota(pcol, [[0, 1]], base=0, channel_multiplier=1,
                           allow_small_or_imprecise_dtypes=True).then_inc(pool_c, 1)
            nc.gpsimd.iota(jcol, [[1, 4]], base=0, channel_multiplier=4,
                           allow_small_or_imprecise_dtypes=True).then_inc(pool_c, 1)
            pool.wait_ge(slots_ready, 1)
            pool.wait_ge(rec_ready, 3)
            pool.wait_ge(filled, 16 * 9)

            def stage_edges(u, h, r):
                for k in range(8):
                    need(pool, sc[8 * h + k], r * 16)
                nc.gpsimd.tensor_copy(stage_i[0:T, h, :], slot_i[0:T, ds(u * 8, 8)]).then_inc(staged, 1)
                nc.gpsimd.tensor_copy(stage_r[0:T, h, :, :], rec[0:T, ds(u * 8, 8), :]).then_inc(staged, 1)
                need(pool, staged, 2 * (u + 1))
                pool.sem_inc(go, 1)
                for k in range(8):
                    pool.indirect_dma_start(io["rec_d"], bass.IndirectOffsetOnAxis(stage_i[0:T, h, k:k + 1], 0),
                                            stage_r[0:T, h, k, :], None).then_inc(sc[8 * h + k], 16)
            over(pool, EC // 8, 2, stage_edges)
            for k in range(2):
                pool.wait_ge(xn_store[k], 16 * len(range(k, NT, 2)))
            pool.wait_ge(recs_in, 16)
            pool.wait_ge(p2_ft, NT)

            def gather_edges(u, h, r):
                need(pool, g_mm, 8 * u - 8)
                nc.gpsimd.tensor_copy(gix[:, h, :], recs[:, ds(u * 8, 8), 0:1].rearrange("p j f -> p (j f)")).then_inc(gix_ready, 1)
                need(pool, gix_ready, u + 1)
                pool.sem_inc(go, 1)
                for k in range(8):
                    pool.indirect_dma_start(ring[:, 8 * h + k, :], None, io["xn_d"],
                                            bass.IndirectOffsetOnAxis(gix[:, h, k:k + 1], 0)).then_inc(gth[8 * h + k], 16)
            over(pool, EB // 8, 2, gather_edges)

            pool.wait_ge(tok_slots, 1)

            def scatter_tokens(t, s, r):
                need(pool, t_st, 2 * (t + 1))
                pool.sem_inc(go, 1)
                for c in range(2):
                    pool.indirect_dma_start(io["xs_d"], bass.IndirectOffsetOnAxis(tix[0:T, s, c:c + 1], 0),
                                            xb[s], None).then_inc(ts[2 * s + c], 16)
            over(pool, NT, 4, scatter_tokens)
            pool.wait_ge(ys_all, 1)

            def gather_tokens(t, s, r):
                need(pool, c_v, 2 * (t - 3))
                nc.gpsimd.tensor_copy(tix[0:T, s, :], slots[0:T, ds(t, 1), :].rearrange("p a b -> p (a b)")).then_inc(c_ix, 1)
                need(pool, c_ix, t + 1)
                pool.sem_inc(go, 1)
                for c in range(2):
                    pool.indirect_dma_start(gel[c][0:T, C * s:C * s + C], None, io["ys_d"],
                                            bass.IndirectOffsetOnAxis(tix[0:T, s, c:c + 1], 0)).then_inc(cg[2 * s + c], 16)
            over(pool, NT, 4, gather_tokens)

        @block.tensor
        def _(pe):
            pe.wait_ge(e_cnt, 1)
            nc.tensor.matmul(ps[0:T, 6, 0:NT], tri[0:T, 0:T], ecnt, start=True, stop=True)
            nc.tensor.matmul(ps[0:T, 7, 0:NT], ones[0:T, 0:T], ecnt, start=True, stop=True).then_inc(e_pre, 1)

            def transposes(t, s, r):
                need(pe, h_ready, t + 1)
                need(pe, tp_evac, 2 * (t - 1))
                for k in range(2):
                    nc.tensor.transpose(ps[:, s, 128 * k:128 * k + T], xnb[s][:, 128 * k:128 * k + 128], ident[0:T, 0:T])
                for k in range(2):
                    mm = nc.tensor.transpose(ps[:, s, 256 + 128 * k:256 + 128 * k + T], hb[s][:, 128 * k:128 * k + 128], ident[0:T, 0:T])
                mm.then_inc(tp_done, 1)
            over(pe, NT, 2, transposes)
            pe.wait_ge(tp_evac, 2 * NT)
            pe.wait_ge(ld_w, 16 * 12)

            def project(i, n):
                for j in range(OC):
                    need(pe, qk_act, OC * (i - 1) + j + 1)
                    for k in range(2):
                        mm = nc.tensor.matmul(ps[:, j, 0:n], wq[:, k, 128 * j:128 * j + 128], HT[:, k, ds(i * TC, n)],
                                              start=(k == 0), stop=(k == 1))
                    mm.then_inc(qk_mm, 1)
            project(0, TC)
            with pe.Fori(1, N // TC) as i:
                project(i, TC)
            project(N // TC, N % TC)

            def channels(slot, h_ap):
                for j in range(OC):
                    nc.tensor.transpose(psf[0:T, 2048 * slot + 128 * j:2048 * slot + 128 * j + 128], h_ap[:, j, :], ident)
                for j in range(OC):
                    mm = nc.tensor.matmul(psf[0:T, 2048 * slot + 1024 + 128 * j:2048 * slot + 1152 + 128 * j],
                                          h_ap[:, j, :], bd[:, j, :], start=True, stop=True)
                return mm

            def pass1(t, s, r):
                need(pe, p1_st, t + 1)
                need(pe, p1_sq, 2 * (t - 1))
                channels(s, hst[s]).then_inc(p1_mm, 1)
            over(pe, NT, 2, pass1)
            pe.wait_ge(p1_sq, 2 * NT)

            def mix_transpose(t, s):
                need(pe, p2_v, 6 * (t + 1))
                need(pe, p2_oT, t - 1)
                for k in range(4):
                    mm = nc.tensor.transpose(ps[:, 4 + s, 128 * k:128 * k + T], o[s][:, 128 * k:128 * k + 128], ident[0:T, 0:T])
                mm.then_inc(p2_tr, 1)

            def mix_out(t, s):
                need(pe, p2_oT, t + 1)
                need(pe, p2_out, t - 1)
                for k in range(4):
                    mm = nc.tensor.matmul(ps[0:T, 6 + s, 0:C], oT[s][:, k, :], wres[:, k, :], start=(k == 0), stop=(k == 3))
                mm.then_inc(p2_ft, 1)

            def pass2(t, s, r):
                need(pe, p2_st, t + 1)
                need(pe, p2_ab, t)
                channels(0, hst[s]).then_inc(p2_mm, 1)
                if not isinstance(t, int) or t >= 1:
                    mix_transpose(t - 1, 1 - s)
                if not isinstance(t, int) or t >= 2:
                    mix_out(t - 2, s)
            over(pe, NT, 2, pass2, peel=2)
            mix_transpose(NT - 1, (NT - 1) % 2)
            mix_out(NT - 2, (NT - 2) % 2)
            mix_out(NT - 1, (NT - 1) % 2)
            pe.wait_ge(p2_out, NT)

            def sum_edges(b, s, r):
                pe.wait_ge(gth[s], 16 * (r + 1))
                need(pe, selm, b + 1)
                need(pe, g_acc, b - 3)
                for k in range(2):
                    mm = nc.tensor.matmul(ps[:, s % 4, 256 * k:256 * k + T], ring[:, s, 128 * k:128 * k + 128],
                                          sel[s % 4], start=True, stop=True)
                mm.then_inc(g_mm, 1)
            over(pe, EB, GR, sum_edges)

            pe.wait_ge(gnn_in, 16)

            def node_products(t, s, r):
                need(pe, n_st, 2 * (t + 1))
                need(pe, n_v, 4 * (t - 1))
                for k in range(4):
                    lhs = gst[s] if k < 2 else gst[2 + s]
                    mm = nc.tensor.matmul(ps[0:T, 4 + s, 0:C], lhs[:, k % 2, :], gnnW[:, k, :], start=(k == 0), stop=(k == 3))
                mm.then_inc(n_mm, 1)
            over(pe, NT, 2, node_products)

            def logits(t, s):
                need(pe, z_T, t + 1)
                for k in range(2):
                    mm = nc.tensor.matmul(ps[0:T, 7, ds(t * NE, NE)], zT[s][:, k, :], Wr[:, k, :], start=(k == 0), stop=(k == 1))
                mm.then_inc(z_lg, 1)

            def token_transposes(t, s, r):
                need(pe, z_ready, t + 1)
                need(pe, z_T, t - 1)
                for k in range(2):
                    mm = nc.tensor.transpose(ps[:, s, 128 * k:128 * k + T], xb[s][:, 128 * k:128 * k + 128], ident[0:T, 0:T])
                mm.then_inc(z_tr, 1)
                if not isinstance(t, int) or t >= 1:
                    logits(t - 1, 1 - s)
            over(pe, NT, 2, token_transposes)
            logits(NT - 1, (NT - 1) % 2)
            pe.wait_ge(routed, 1)
            nc.tensor.matmul(ps[0:T, 0, 0:200], tri[0:T, 0:T], msum, start=True, stop=True)
            nc.tensor.matmul(ps[0:T, 1, 0:200], ones[0:T, 0:T], msum, start=True, stop=True).then_inc(prefixed, 1)

            pe.wait_ge(w1_in, 16 * NE)
            pe.wait_ge(w2_in, 16 * NE)
            pe.wait_ge(b3_in, 48)
            pe.wait_ge(tok_slots, 1)

            def ex_x(b, s, r):
                pe.wait_ge(xs_in[s], 16 * (r + 1))
                need(pe, m_xe, 2 * b)
                for k in range(2):
                    mm = nc.tensor.transpose(ps[:, 6, 128 * k:128 * k + 128], xsb[s][:, 128 * k:128 * k + 128], ident)
                mm.then_inc(m_xt, 1)

            def ex_1(b, s):
                need(pe, m_xe, 2 * (b + 1))
                need(pe, m_w1, b + 1)
                need(pe, m_ge, b - 1)
                for j in range(8):
                    for k in range(2):
                        mm = nc.tensor.matmul(psf[:, 1024 * s + 128 * j:1024 * s + 128 * j + 128],
                                              W1b[s][:, k, 128 * j:128 * j + 128], xeT[s][:, k, :],
                                              start=(k == 0), stop=(k == 1))
                mm.then_inc(m_g1, 1)

            def ex_2(b, s, e):
                need(pe, m_ge, b + 1)
                need(pe, m_y, b - 1)
                out = ps[:, 4 + s, 0:C]
                nc.tensor.matmul(out, ones3[0:3, :], b2s[:, ds(e, 1), :], start=True, stop=False)
                for k in range(8):
                    mm = nc.tensor.matmul(out, gel[s][:, 128 * k:128 * k + 128], W2[:, ds(e, 1), k, :], start=False, stop=(k == 7))
                mm.then_inc(m_g2, 1)

            def expert_of(b):
                return pe.value_load(expert_row[0:1, ds(b, 1)], min_val=0, max_val=NE - 1)

            ex_x(0, 0, 0)

            def experts(b, s, r):
                ex_1(b, s % 2)
                if not isinstance(b, int) or b + 1 < TB:
                    ex_x(b + 1, (s + 1) % 4, r + (s + 1) // 4)
                if not isinstance(b, int) or b >= 1:
                    ex_2(b - 1, (s + 1) % 2, expert_of(b - 1))
            over(pe, TB, 4, experts, ahead=1)
            ex_2(TB - 1, (TB - 1) % 2, expert_of(TB - 1))

        @block.scalar
        def _(act):
            act.wait_ge(row_in, 1)
            nc.scalar.activation(nrm, tmpa, ACT.Sqrt).then_inc(row_out, 1)
            act.wait_ge(row_in, 2)
            nc.scalar.activation(tmpb, tmpa, ACT.Sqrt).then_inc(row_out, 1)
            act.wait_ge(row_in, 3)
            nc.scalar.activation(tmpc, tmpa, ACT.Ln).then_inc(row_out, 1)
            act.wait_ge(filled, 16 * 9)
            act.wait_ge(rec_ready, 3)
            act.wait_ge(tile_row_in, 16)

            def tp_out(t, s, r):
                need(act, tp_done, t + 1)
                act.sem_inc(act_go, 1)
                nc.scalar.activation(XNT[:, :, ds(t * T, T)], ps[:, s, 0:256].rearrange("p (k n) -> p k n", k=2)[:, :, 0:T],
                                     ACT.Copy).then_inc(tp_evac, 1)
                nc.scalar.activation(HT[:, :, ds(t * T, T)], ps[:, s, 256:512].rearrange("p (k n) -> p k n", k=2)[:, :, 0:T],
                                     ACT.Copy).then_inc(tp_evac, 1)
            over(act, NT, 2, tp_out)

            def project_out(i, n):
                for j in range(OC):
                    need(act, qk_mm, OC * i + j + 1)
                    act.sem_inc(act_go, 1)
                    nc.scalar.activation(HC[:, j, ds(i * TC, n)], ps[:, j, 0:n], ACT.Copy).then_inc(qk_act, 1)
            act.wait_ge(slots_ready, 1)
            project_out(0, TC)
            with act.Fori(1, N // TC) as i:
                project_out(i, TC)
            project_out(N // TC, N % TC)
            act.wait_ge(row_in, 4)
            nc.scalar.activation(bnt, bnt, ACT.Sqrt).then_inc(row_out, 1)
            act.wait_ge(bn_ready, 1)
            for j in range(OC):
                nc.scalar.activation(HC[:, j, :], HC[:, j, :], ACT.Relu, bias=bnb[:, j:j + 1],
                                     scale=bna[:, j:j + 1]).then_inc(hc_ready, 1)

            def squares(t, s, r):
                need(act, p1_mm, t + 1)
                act.sem_inc(act_go, 1)
                h2 = psf[0:T, 2048 * s:2048 * s + Q3]
                s2 = psf[0:T, 2048 * s + 1024:2048 * s + 1024 + Q3]
                nc.scalar.activation(h2, h2, ACT.Square,
                                     accum_out=sq_h[:, ds(t, 1)]).then_inc(p1_sq, 1)
                nc.scalar.activation(s2, s2, ACT.Square,
                                     accum_out=sq_s[:, ds(t, 1)]).then_inc(p1_sq, 1)
            over(act, NT, 2, squares)
            act.wait_ge(row_in, 5)
            nc.scalar.activation(tmpa, sq_h, ACT.Sqrt)
            nc.scalar.activation(tmpb, tmpb, ACT.Sqrt).then_inc(row_out, 1)

            def mix_copy(t, s):
                need(act, p2_tr, t + 1)
                need(act, p2_ft, t - 1)
                act.sem_inc(act_go, 1)
                nc.scalar.activation(oT[s], ps[:, 4 + s, :].rearrange("p (k n) -> p k n", k=4)[:, :, 0:T], ACT.Copy).then_inc(p2_oT, 1)
                need(act, p2_sq, t - 1)
                nc.scalar.activation(junk[s], o[s], ACT.Square, accum_out=o2[:, ds(t, 1)]).then_inc(p2_sq, 1)

            def mix_store(t, s):
                need(act, p2_ft, t + 1)
                act.sem_inc(act_go, 1)
                nc.scalar.activation(HC[0:T, 0:4, ds(t * T, C // 4)], ps[0:T, 6 + s, 0:C].rearrange("p (q c) -> p q c", q=4), ACT.Copy).then_inc(p2_out, 1)

            def mix_in(t, s, r):
                need(act, p2_mm, t + 1)
                need(act, p2_v, 6 * (t - 1))
                act.sem_inc(act_go, 1)
                a = ab[s]
                nc.scalar.activation(a[:, 0:Q3], psf[0:T, 0:Q3], ACT.Copy)
                v_out = a[:, Q3:].rearrange("p (g c) -> p g c", g=8)
                v_in = psf[0:T, 1024:1024 + Q3].rearrange("p (g c) -> p g c", g=8)
                nc.scalar.activation(v_out[:, :, 0:64], v_in[:, :, 0:64], ACT.Relu)
                nc.scalar.activation(v_out[:, :, 64:96], v_in[:, :, 64:96], ACT.Copy).then_inc(p2_ab, 1)
                if not isinstance(t, int) or t >= 1:
                    mix_copy(t - 1, 1 - s)
                if not isinstance(t, int) or t >= 2:
                    mix_store(t - 2, s)
            over(act, NT, 2, mix_in, peel=2)
            mix_copy(NT - 1, (NT - 1) % 2)
            mix_store(NT - 2, (NT - 2) % 2)
            mix_store(NT - 1, (NT - 1) % 2)
            act.wait_ge(p2_sq, NT)
            nc.scalar.activation(tmpa, o2, ACT.Sqrt).then_inc(row_out, 1)

            def out_norm(t, s, r):
                need(act, ft_ready, t + 1)
                need(act, f2_ready, t - 1)
                act.sem_inc(act_go, 1)
                nc.scalar.activation(junk[s][:, 0:C].rearrange("p (q c) -> p q c", q=4), HC[0:T, 0:4, ds(t * T, C // 4)], ACT.Square,
                                     accum_out=f2[:, ds(t, 1)]).then_inc(f2_ready, 1)
            over(act, NT, 2, out_norm)
            act.wait_ge(f2_ready, NT)
            nc.scalar.activation(tmpa, f2, ACT.Sqrt).then_inc(row_out, 1)
            act.wait_ge(row_in, 6)
            nc.scalar.activation(tmpb, tmpa, ACT.Tanh).then_inc(row_out, 1)

            act.wait_ge(row_in, 7)
            nc.scalar.activation(tmpb, tmpa, ACT.Sqrt).then_inc(row_out, 1)
            act.wait_ge(row_in, 8)
            nc.scalar.activation(tmpb, tmpa, ACT.Sqrt).then_inc(row_out, 1)

            def z_copy(t, s, r):
                need(act, z_tr, t + 1)
                need(act, z_lg, t - 1)
                act.sem_inc(act_go, 1)
                nc.scalar.activation(zT[s], ps[:, s, 0:256].rearrange("p (k n) -> p k n", k=2)[:, :, 0:T], ACT.Copy).then_inc(z_T, 1)
            over(act, NT, 2, z_copy)
            act.wait_ge(row_in, 9)
            nc.scalar.activation(e21, e21, ACT.Exp).then_inc(row_out, 1)

            def gelu(b, s, r):
                need(act, m_g1, b + 1)
                need(act, m_gb, 3 * (b + 1))
                need(act, m_g2, b - 1)
                for j in range(8):
                    ins = nc.scalar.activation(gel[s][:, 128 * j:128 * j + 128],
                                               psf[:, 1024 * s + 128 * j:1024 * s + 128 * j + 128], ACT.Gelu,
                                               bias=b1c[s][:, j:j + 1])
                ins.then_inc(m_ge, 1)
                if not isinstance(b, int) or b >= 1:
                    y_copy(b - 1, 1 - s, r + s - 1)

            def y_copy(b, s, r):
                need(act, m_g2, b + 1)
                need(act, ys_out[s], 16 * r)
                nc.scalar.activation(ysb[s], ps[:, 4 + s, 0:C], ACT.Copy).then_inc(m_y, 1)
            over(act, TB, 2, gelu, peel=2)
            y_copy(TB - 1, (TB - 1) % 2, (TB - 1) // 2)

        @block.vector
        def _(v):
            V = nc.vector
            count = [0]

            def chain(ins):
                count[0] += 1
                ins.then_inc(dve_step, 1)
                v.wait_ge(dve_step, count[0])

            V.memset(zero, 0.0).then_inc(zeroed, 1)
            V.memset(bd, 0.0).then_inc(zeroed, 1)
            V.memset(ones, 1.0)
            V.memset(ones3, 1.0)
            v.wait_ge(pool_c, 3)
            V.tensor_scalar(tri, iota, pcol, None, ALU.is_gt)
            chain(V.tensor_scalar(ident, iota, pcol, None, ALU.is_equal))

            v.wait_ge(ld_edges, 48)
            chain(V.tensor_copy(src_f, src_i))
            chain(V.tensor_scalar(e1, src_f, 1.0 / T, 0.5 / T - 0.5, ALU.mult, ALU.add))
            chain(V.tensor_scalar(tile_f, e1, ROUND, -ROUND, ALU.add, ALU.add))
            V.tensor_copy(rec[0:T, :, 0], dst_i).then_inc(rec_ready, 1)
            V.scalar_tensor_tensor(rec[0:T, :, 1], tile_f, -float(T), src_f, ALU.mult, ALU.add).then_inc(rec_ready, 1)
            V.tensor_copy(rec[0:T, :, 3], w_e)
            V.tensor_copy(rec[0:T, :, 2], w_e).then_inc(rec_ready, 1)
            chain(V.tensor_tensor(member, tile_f.unsqueeze(1).to_broadcast([T, NT, EC]),
                                  iota[0:T, 0:NT].unsqueeze(2).to_broadcast([T, NT, EC]), ALU.is_equal))
            rank_f = rank.rearrange("p t c -> p (t c)")
            member_f = member.rearrange("p t c -> p (t c)")
            chain(V.tensor_tensor_scan(rank_f, member_f, member_f, 0.0, ALU.add, ALU.max))
            V.tensor_copy(ecnt[:, 0:1], rank[:, 0:1, EC - 1])
            V.tensor_tensor(ecnt[:, 1:NT], rank[:, 1:NT, EC - 1], rank[:, 0:NT - 1, EC - 1], ALU.subtract).then_inc(e_cnt, 1)
            v.wait_ge(e_pre, 1)
            V.tensor_copy(epre, ps[0:T, 6, 0:NT])
            chain(V.tensor_copy(etot, ps[0:T, 7, 0:NT]))
            chain(V.tensor_scalar(eblk, etot, 1.0 / 128, CEIL, ALU.mult, ALU.add))
            chain(V.tensor_scalar(eblk, eblk, ROUND, -ROUND, ALU.add, ALU.add))
            chain(V.tensor_tensor_scan(ebcum, eblk, eblk, 0.0, ALU.add, ALU.max))
            chain(V.tensor_tensor(eadj, ebcum, eblk, ALU.subtract))
            chain(V.scalar_tensor_tensor(eadj, eadj, 128.0, epre, ALU.mult, ALU.add))
            chain(V.tensor_scalar(eadj, eadj, -1.0, None, ALU.add))
            chain(V.tensor_tensor(eadj[:, 1:NT], eadj[:, 1:NT], rank[:, 0:NT - 1, EC - 1], ALU.subtract))
            for t in range(NT):
                place = V.scalar_tensor_tensor(rank[:, t, :], rank[:, t, :], eadj[:, t:t + 1], member[:, t, :],
                                               ALU.add, ALU.mult)
            chain(place)
            chain(V.tensor_reduce(e1, rank.rearrange("p t c -> p c t"), AX, ALU.add))
            chain(V.tensor_scalar(e2, e1, 1.0 / 128, FLOOR, ALU.mult, ALU.add))
            chain(V.tensor_scalar(e2, e2, ROUND, -ROUND, ALU.add, ALU.add))
            chain(V.scalar_tensor_tensor(e1, e2, -128.0, e1, ALU.mult, ALU.add))
            V.scalar_tensor_tensor(slot_i[0:T, :], e1, float(EB), e2, ALU.mult, ALU.add).then_inc(slots_ready, 1)
            nb = EB // 4
            chain(V.tensor_tensor(ecmp, jcol[0:nb, :].unsqueeze(2).to_broadcast([nb, 4, NT]),
                                  ebcum[0:nb, :].unsqueeze(1).to_broadcast([nb, 4, NT]), ALU.is_ge))
            chain(V.tensor_reduce(etile, ecmp, AX, ALU.add))
            chain(V.tensor_scalar(etile, etile, NT - 1.0, None, ALU.min))
            chain(V.tensor_copy(epack, etile[:, 3:4]))
            for q in (2, 1):
                chain(V.scalar_tensor_tensor(epack, epack, 32.0, etile[:, q:q + 1], ALU.mult, ALU.add))
            V.scalar_tensor_tensor(etile_i, epack, 32.0, etile[:, 0:1], ALU.mult, ALU.add).then_inc(etile_ready, 1)

            def layer_stats(t, s, r):
                V.bn_stats(stats[:, ds(t, 1), :].rearrange("p a k -> p (a k)"),
                           X[0:T, ds(t, 1), :].rearrange("p a c -> p (a c)")).then_inc(st_done, 1)

            def layer_aggr():
                for t in range(NT):
                    last = V.bn_aggr(mv[:, t, :], stats[:, t, :])
                return last
            v.wait_ge(ld_x, 16)
            over(v, NT, 5, layer_stats)
            v.wait_ge(st_done, NT)
            chain(layer_aggr())
            V.tensor_scalar(tmpa, var_, LN_EPS, None, ALU.add).then_inc(row_in, 1)
            v.wait_ge(row_out, 1)
            chain(V.reciprocal(rstd, nrm))
            chain(V.tensor_tensor(tmpa, var_, rstd, ALU.mult))
            V.scalar_tensor_tensor(tmpa, tmpa, float(C), rstd, ALU.mult, ALU.mult).then_inc(row_in, 1)
            v.wait_ge(row_out, 2)
            chain(V.tensor_scalar(nrm, tmpb, MIN_NORM, None, ALU.max))
            chain(V.tensor_scalar(tmpb, nrm, MAXNORM, None, ALU.min))
            V.tensor_scalar(cc_, tmpb, -1.0, 1.0, ALU.mult, ALU.add)
            chain(V.tensor_scalar(tmpa, tmpb, 1.0, None, ALU.add))
            chain(V.reciprocal(cc_, cc_))
            V.tensor_tensor(tmpa, tmpa, cc_, ALU.mult).then_inc(row_in, 1)
            chain(V.tensor_tensor(sq_h, tmpb, tmpb, ALU.mult))
            chain(V.tensor_scalar(sq_s, sq_h, 0.2, 1.0 / 3, ALU.mult, ALU.add))
            chain(V.tensor_tensor(sq_s, sq_s, sq_h, ALU.mult))
            chain(V.tensor_scalar(sq_s, sq_s, 1.0, None, ALU.add))
            chain(V.reciprocal(nrm, nrm))
            v.wait_ge(row_out, 3)
            chain(V.scalar_tensor_tensor(s1, tmpc, 0.5, nrm, ALU.mult, ALU.mult))
            chain(V.tensor_tensor(sq_s, sq_s, s1, ALU.subtract))
            chain(V.tensor_scalar(tmpb, tmpb, 0.05, None, ALU.is_lt))
            chain(V.tensor_tensor(sq_s, sq_s, tmpb, ALU.mult))
            chain(V.tensor_tensor(s1, s1, sq_s, ALU.add))

            def normalise(t, s, r):
                need(v, xn_store[s], 16 * r)
                need(v, tp_done, t - 1)
                V.tensor_scalar(xnb[s], X[0:T, ds(t, 1), :].rearrange("p a c -> p (a c)"), mean_[:, ds(t, 1)],
                                rstd[:, ds(t, 1)], ALU.subtract, ALU.mult).then_inc(xn_ready, 1)
                need(v, xn_ready, t + 1)
                V.tensor_scalar(hb[s], xnb[s], s1[:, ds(t, 1)], None, ALU.mult).then_inc(h_ready, 1)
            over(v, NT, 2, normalise)

            def project_stats(i, n):
                for j in range(OC):
                    need(v, qk_act, OC * i + j + 1)
                    V.bn_stats(bst[:, j, ds(i, 1), :].rearrange("p a k -> p (a k)"), HC[:, j, ds(i * TC, n)]).then_inc(qk_dve, 1)
            project_stats(0, TC)
            with v.Fori(1, N // TC) as i:
                project_stats(i, TC)
            project_stats(N // TC, N % TC)
            v.wait_ge(qk_dve, OC * 7)
            for j in range(OC):
                ins = V.bn_aggr(bmv[:, j, :], bst[:, j, :, :].rearrange("p i k -> p (i k)"))
            chain(ins)
            v.wait_ge(ld_w, 16 * 12)
            V.tensor_scalar(bnt, bmv[:, :, 1], 1e-5, None, ALU.add).then_inc(row_in, 1)
            v.wait_ge(ld_bd, 64)
            for j in range(OC):
                ins = V.tensor_scalar(bd[:, j, :], bd[:, j, :], dw[:, j:j + 1], None, ALU.mult)
            ins.then_inc(bd_ready, 1)
            v.wait_ge(row_out, 4)
            chain(V.reciprocal(bna, bnt))
            chain(V.tensor_tensor(bna, bna, gamma, ALU.mult))
            chain(V.tensor_tensor(bnb, bmv[:, :, 0], bna, ALU.mult))
            V.tensor_tensor(bnb, beta, bnb, ALU.subtract).then_inc(bn_ready, 1)

            v.wait_ge(hc_ready, OC)

            def stage1(t, s, r):
                need(v, p1_mm, t - 1)
                V.tensor_copy(hst[s], HC[:, :, ds(t * T, T)]).then_inc(p1_st, 1)
            over(v, NT, 2, stage1)
            v.wait_ge(p1_sq, 2 * NT)
            V.tensor_tensor(tmpb, sq_h, sq_s, ALU.add).then_inc(row_in, 1)
            v.wait_ge(row_out, 5)
            chain(V.tensor_scalar(tmpa, tmpa, MIN_NORM, None, ALU.max))
            chain(V.reciprocal(tmpa, tmpa))
            chain(V.tensor_scalar(tmpa, tmpa, REACH, 1.0, ALU.mult, ALU.min))
            chain(V.tensor_tensor(tmpb, tmpb, tmpa, ALU.mult))
            chain(V.tensor_scalar(tmpb, tmpb, MIN_NORM, None, ALU.max))
            chain(V.reciprocal(tmpb, tmpb))
            chain(V.tensor_scalar(tmpb, tmpb, REACH, 1.0, ALU.mult, ALU.min))
            chain(V.tensor_tensor(cc_, tmpa, tmpb, ALU.mult))
            chain(V.reciprocal(epsc, cc_))
            chain(V.tensor_scalar(epsc, epsc, ATT_EPS, None, ALU.mult))
            v.wait_ge(filled, 16 * 9)

            def stage2(t, s):
                need(v, p2_mm, t - 1)
                V.tensor_copy(hst[s], HC[:, :, ds(t * T, T)]).then_inc(p2_st, 1)
            stage2(0, 0)

            def attention(t, s, r):
                if not isinstance(t, int) or t + 1 < NT:
                    stage2(t + 1, 1 - s)
                g = ab[s].rearrange("p (g c) -> p g c", g=NG)
                q_, k_, v_ = g[:, :, 0:32], g[:, :, 32:64], g[:, :, 64:96]
                d3, r3, u3, o3 = [a.rearrange("p (g c) -> p g c", g=NG) for a in (den, rden, vr, o[s])]
                need(v, p2_ab, t + 1)
                need(v, p2_v, 6 * t)
                V.tensor_scalar(d3, v_, epsc[:, ds(t, 1)], None, ALU.add).then_inc(p2_v, 1)
                V.tensor_reduce(ksum, k_, AX, ALU.add).then_inc(p2_v, 1)
                need(v, p2_v, 6 * t + 1)
                V.reciprocal(rden, den).then_inc(p2_v, 1)
                need(v, p2_v, 6 * t + 3)
                V.tensor_tensor(u3, r3, v_, ALU.mult).then_inc(p2_v, 1)
                need(v, p2_v, 6 * t + 4)
                V.tensor_tensor(d3, u3, q_, ALU.mult).then_inc(p2_v, 1)
                need(v, p2_v, 6 * t + 5)
                need(v, p2_tr, t - 1)
                need(v, p2_sq, t - 1)
                V.tensor_tensor(o3, d3, ksum.unsqueeze(2).to_broadcast([T, NG, 32]), ALU.mult).then_inc(p2_v, 1)
            over(v, NT, 2, attention, ahead=1)
            v.wait_ge(row_out, 6)
            chain(V.tensor_tensor(cc_, cc_, cc_, ALU.mult))
            chain(V.tensor_tensor(tmpa, tmpa, cc_, ALU.mult))
            chain(V.tensor_scalar(tmpa, tmpa, MIN_NORM, None, ALU.max))
            chain(V.reciprocal(tmpa, tmpa))
            chain(V.tensor_scalar(tmpa, tmpa, REACH, 1.0, ALU.mult, ALU.min))
            chain(V.tensor_tensor(cc_, cc_, tmpa, ALU.mult))
            v.wait_ge(p2_out, NT)
            bres4 = bres.rearrange("p (q c) -> p q c", q=4)

            def project_bias(t, s, r):
                f = HC[0:T, 0:4, ds(t * T, C // 4)]
                V.scalar_tensor_tensor(f, f, cc_[:, ds(t, 1)], bres4, ALU.mult, ALU.add).then_inc(ft_ready, 1)
            over(v, NT, 2, project_bias)
            V.memset(S, 0.0)
            v.wait_ge(row_out, 7)
            V.tensor_scalar(tmpa, tmpa, MIN_NORM, None, ALU.max).then_inc(row_in, 1)
            v.wait_ge(row_out, 8)
            chain(V.reciprocal(tmpa, tmpa))
            chain(V.tensor_scalar(tmpb, tmpb, MAXNORM, None, ALU.min))
            chain(V.tensor_tensor(tmpb, tmpb, tmpa, ALU.mult))
            v.wait_ge(ft_ready, NT)
            X4 = X[0:T, :, :].rearrange("p t (q c) -> p t q c", q=4)

            def add_mixing(t, s, r):
                xt = X4[:, ds(t, 1), :, :].rearrange("p a q c -> p (a q) c")
                V.scalar_tensor_tensor(xt, HC[0:T, 0:4, ds(t * T, C // 4)], tmpb[:, ds(t, 1)], xt,
                                       ALU.mult, ALU.add).then_inc(mix_added, 1)
            over(v, NT, 2, add_mixing)
            v.wait_ge(mix_added, NT)
            v.sem_inc(mixed, 1)
            v.wait_ge(b_in, 16)
            chain(V.tensor_copy(bhi, b2f))
            chain(V.tensor_tensor(b2f, b2f, bhi, ALU.subtract))
            chain(V.tensor_copy(bmid, b2f))
            chain(V.tensor_tensor(b2f, b2f, bmid, ALU.subtract))
            V.tensor_copy(blo, b2f).then_inc(b_split, 1)

            v.wait_ge(recs_in, 16)
            v.wait_ge(tile_row_in, 16)

            def select(b, s):
                need(v, g_mm, b - 3)
                V.tensor_scalar(sel[s], iota[:, 0:T], recs[:, ds(b, 1), 1:2].rearrange("p a f -> p (a f)"),
                                recs[:, ds(b, 1), 2:3].rearrange("p a f -> p (a f)"), ALU.is_equal, ALU.mult).then_inc(selm, 1)
            for b in range(3):
                select(b, b)

            packed = [0]

            def add_sums(b, s, r):
                if not isinstance(b, int) or b + 3 < EB:
                    select(b + 3, (s + 3) % 4)
                if s == 0:
                    packed[0] = v.value_load(tile_row[0:1, ds(r, 1)], min_val=0, max_val=32 ** 4 - 1)
                first = nc.s_assert_within((packed[0] >> 5 * s) & 31, 0, NT - 1,
                                           skip_runtime_bounds_check_because="each digit is clipped to NT - 1") * T
                need(v, g_acc, b)
                need(v, g_mm, b + 1)
                part = SUP[:, :, ds(first, T)]
                V.tensor_tensor(part, part, ps[:, s, :].rearrange("p (k n) -> p k n", k=2)[:, :, 0:T], ALU.add).then_inc(g_acc, 1)
            over(v, EB, 4, add_sums, ahead=3)
            v.wait_ge(g_acc, EB)

            def stage_nodes(t, s):
                need(v, n_mm, t - 1)
                V.tensor_copy(gst[s], XNT[:, :, ds(t * T, T)]).then_inc(n_st, 1)
                V.tensor_copy(gst[2 + s], SUP[:, :, ds(t * T, T)]).then_inc(n_st, 1)
            stage_nodes(0, 0)

            def nodes(t, s, r):
                if not isinstance(t, int) or t + 1 < NT:
                    stage_nodes(t + 1, 1 - s)
                need(v, n_mm, t + 1)
                V.tensor_tensor(xb[s], ps[0:T, 4 + s, 0:C], bg[0:T, :], ALU.add).then_inc(n_v, 1)
                need(v, n_v, 4 * t + 1)
                xt = X[0:T, ds(t, 1), :].rearrange("p a c -> p (a c)")
                V.scalar_tensor_tensor(xt, xb[s], 0.0, xt, ALU.max, ALU.add).then_inc(n_v, 1)
                need(v, n_v, 4 * t + 2)
                V.bn_stats(stats[:, ds(t, 1), :].rearrange("p a k -> p (a k)"), xt).then_inc(n_v, 2)
            over(v, NT, 2, nodes, ahead=1)
            v.wait_ge(n_v, 4 * NT)
            chain(layer_aggr())
            V.tensor_scalar(tmpa, var_, LN_EPS, None, ALU.add).then_inc(row_in, 1)
            v.wait_ge(row_out, 9)
            chain(V.reciprocal(rstd, tmpb))
            chain(V.tensor_tensor(tmpa, var_, rstd, ALU.mult))
            chain(V.tensor_tensor(tmpa, tmpa, rstd, ALU.mult))
            V.tensor_scalar(tmpa, tmpa, LN_EPS, None, ALU.add).then_inc(row_in, 1)
            v.wait_ge(row_out, 10)
            chain(V.reciprocal(rstd2, tmpb))
            chain(V.tensor_tensor(rstd2, rstd2, rstd, ALU.mult))

            def normalise2(t, s, r):
                need(v, z_tr, t - 1)
                V.tensor_scalar(xb[s], X[0:T, ds(t, 1), :].rearrange("p a c -> p (a c)"), mean_[:, ds(t, 1)],
                                rstd[:, ds(t, 1)], ALU.subtract, ALU.mult).then_inc(z_ready, 1)
            over(v, NT, 2, normalise2)

            v.wait_ge(z_lg, NT)
            chain(V.tensor_tensor(lg, ps[0:T, 7, 0:NT * NE].rearrange("p (t e) -> p t e", t=NT),
                                  br[0:T, :].unsqueeze(1).to_broadcast([T, NT, NE]), ALU.add))
            eidx = iota[0:T, 0:NE].unsqueeze(1).to_broadcast([T, NT, NE])

            def best(values, m, idx, hot):
                chain(V.tensor_reduce(m, values, AX, ALU.max))
                chain(V.tensor_tensor(t1, values, m.unsqueeze(2).to_broadcast([T, NT, NE]), ALU.is_equal))
                chain(V.tensor_scalar(t1, t1, -100.0, 100.0, ALU.mult, ALU.add))
                chain(V.tensor_tensor(t1, t1, eidx, ALU.add))
                chain(V.tensor_reduce(idx, t1, AX, ALU.min))
                chain(V.tensor_tensor(hot, eidx, idx.unsqueeze(2).to_broadcast([T, NT, NE]), ALU.is_equal))
            best(lg, m1, i1, oh1)
            chain(V.scalar_tensor_tensor(cand, oh1, -3e38, lg, ALU.mult, ALU.add))
            best(cand, m2, i2, oh2)
            V.tensor_tensor(e21, m2, m1, ALU.subtract).then_inc(row_in, 1)
            V.tensor_tensor(msum.rearrange("p (e t) -> p t e", e=NE), oh1, oh2, ALU.add).then_inc(routed, 1)

            v.wait_ge(prefixed, 1)
            chain(V.tensor_copy(tot, ps[0:T, 1, 0:200]))
            chain(V.tensor_tensor_scan(cs, tot, tot, 0.0, ALU.add, ALU.max))
            last = cs.rearrange("p (e t) -> p e t", e=NE)[:, :, NT - 1]
            chain(V.tensor_copy(bexp, last))
            chain(V.tensor_tensor(bexp[:, 1:NE], last[:, 1:NE], last[:, 0:NE - 1], ALU.subtract))
            chain(V.tensor_scalar(bexp, bexp, 1.0 / 128, CEIL, ALU.mult, ALU.add))
            chain(V.tensor_scalar(bexp, bexp, ROUND, -ROUND, ALU.add, ALU.add))
            chain(V.tensor_tensor_scan(bend, bexp, bexp, 0.0, ALU.add, ALU.max))
            chain(V.tensor_tensor(adj8, bend, bexp, ALU.subtract))
            chain(V.tensor_scalar(adj8, adj8, 128.0, None, ALU.mult))
            chain(V.tensor_tensor(adj8[:, 1:NE], adj8[:, 1:NE], last[:, 0:NE - 1], ALU.subtract))
            chain(V.tensor_tensor(pos, cs, tot, ALU.subtract))
            chain(V.tensor_tensor(pos, pos, ps[0:T, 0, 0:200], ALU.add))
            pos_te = pos.rearrange("p (e t) -> p t e", e=NE)
            chain(V.tensor_tensor(cand, pos_te, adj8.unsqueeze(1).to_broadcast([T, NT, NE]), ALU.add))
            V.tensor_tensor(t1, cand, oh1, ALU.mult)
            chain(V.tensor_tensor(t2, cand, oh2, ALU.mult))
            V.tensor_reduce(sl[:, :, 0], t1, AX, ALU.add)
            chain(V.tensor_reduce(sl[:, :, 1], t2, AX, ALU.add))
            chain(V.tensor_copy(slots[0:T, :, :], sl))
            chain(V.tensor_tensor(bcmp, iota[0:1, 0:TB].unsqueeze(2).to_broadcast([1, TB, NE]),
                                  bend[0:1, :].unsqueeze(1).to_broadcast([1, TB, NE]), ALU.is_ge))
            chain(V.tensor_reduce(brow, bcmp, AX, ALU.add))
            chain(V.tensor_scalar(expert_row[0:1, :], brow, NE - 1.0, None, ALU.min))
            v.wait_ge(row_out, 11)
            chain(V.tensor_scalar(den1, e21, 1.0, None, ALU.add))
            chain(V.reciprocal(wgt1, den1))
            chain(V.tensor_tensor(wgt2, wgt1, e21, ALU.mult))
            v.sem_inc(tok_slots, 1)

            def stage_tokens(t, s, r):
                for c in range(2):
                    need(v, ts[2 * s + c], 16 * r)
                V.tensor_copy(tix[0:T, s, :], slots[0:T, ds(t, 1), :].rearrange("p a b -> p (a b)")).then_inc(t_st, 1)
                V.tensor_scalar(xb[s], X[0:T, ds(t, 1), :].rearrange("p a c -> p (a c)"), mean_[:, ds(t, 1)],
                                rstd2[:, ds(t, 1)], ALU.subtract, ALU.mult).then_inc(t_st, 1)
            over(v, NT, 4, stage_tokens)

            def expert_in(b, s):
                e = v.value_load(expert_row[0:1, ds(b, 1)], min_val=0, max_val=NE - 1)
                need(v, m_g1, b - 1)
                need(v, m_ge, b - 1)
                need(v, m_xe, 2 * b)
                v.sem_inc(dve_go, 1)
                V.tensor_copy(W1b[s], W1[:, ds(e, 1), :, :].rearrange("p e k h -> p (e k) h")).then_inc(m_w1, 1)
                V.tensor_copy(gcol, lng[:, :, ds(e, 1)].rearrange("p k e -> p (k e)")).then_inc(m_gb, 1)
                V.tensor_copy(bcol, lnb[:, :, ds(e, 1)].rearrange("p k e -> p (k e)")).then_inc(m_gb, 1)
                V.tensor_copy(b1c[s], b1T[:, :, ds(e, 1)].rearrange("p k e -> p (k e)")).then_inc(m_gb, 1)
                need(v, m_xt, b + 1)
                need(v, m_gb, 3 * (b + 1))
                for k in range(2):
                    V.tensor_scalar(xeT[s][:, k, :], ps[:, 6, 128 * k:128 * k + 128], gcol[:, k:k + 1],
                                    bcol[:, k:k + 1], ALU.mult, ALU.add).then_inc(m_xe, 1)
            v.wait_ge(w1_in, 16 * NE)
            expert_in(0, 0)

            def expert_v(b, s, r):
                if not isinstance(b, int) or b + 1 < TB:
                    expert_in(b + 1, 1 - s)
            over(v, TB, 2, expert_v, ahead=1)

            def combine(t, s, r):
                v.wait_ge(cg[2 * s], 16 * (r + 1))
                need(v, out_st[s], 16 * r)
                V.scalar_tensor_tensor(xb[s], gel[0][0:T, C * s:C * s + C], wgt1[:, ds(t, 1)],
                                       X[0:T, ds(t, 1), :].rearrange("p a c -> p (a c)"), ALU.mult, ALU.add).then_inc(c_v, 1)
                v.wait_ge(cg[2 * s + 1], 16 * (r + 1))
                need(v, c_v, 2 * t + 1)
                V.scalar_tensor_tensor(xb[s], gel[1][0:T, C * s:C * s + C], wgt2[:, ds(t, 1)], xb[s],
                                       ALU.mult, ALU.add).then_inc(c_v, 1)
            over(v, NT, 4, combine)


INPUTS = ["x", "src", "dst", "edge_weight", "gnn_W", "gnn_b", "w_qT", "bn_gamma", "bn_beta", "w_dw", "w_pwT",
          "w_resT", "b_res", "Wr", "br", "ln_gT", "ln_bT", "W1", "b1T", "W2", "b2"]


def kernel(x, src, dst, edge_weight, L0_gnn_W, L0_gnn_b, L0_mix_w_qkv, L0_mix_bn_gamma, L0_mix_bn_beta,
           L0_mix_w_dw, L0_mix_w_pw, L0_mix_w_res, L0_mix_b_res, L0_ffn_Wr, L0_ffn_br, L0_ffn_ln_g,
           L0_ffn_ln_b, L0_ffn_W1, L0_ffn_b1, L0_ffn_W2, L0_ffn_b2):
    import concourse.bacc as bacc
    from concourse.bass_utils import run_bass_kernel_spmd

    def by_chunk(a):
        return np.asarray(a).reshape(OC, 128).T

    values = [x, src, dst, edge_weight, L0_gnn_W, L0_gnn_b, np.asarray(L0_mix_w_qkv)[:, :, 2].T,
              by_chunk(L0_mix_bn_gamma), by_chunk(L0_mix_bn_beta), by_chunk(np.asarray(L0_mix_w_dw)[:, 0, 2]), np.asarray(L0_mix_w_pw)[:, :, 0].T,
              np.asarray(L0_mix_w_res)[:, :, 0].T, L0_mix_b_res, L0_ffn_Wr, L0_ffn_br,
              np.asarray(L0_ffn_ln_g).T, np.asarray(L0_ffn_ln_b).T, L0_ffn_W1,
              np.asarray(L0_ffn_b1).reshape(NE, 8, 128).transpose(2, 1, 0), L0_ffn_W2, L0_ffn_b2]
    nc = bacc.Bacc("TRN2", target_bir_lowering=False, num_devices=1)
    arrays, io = {}, {}
    for name, value in zip(INPUTS, values):
        a = np.ascontiguousarray(value)
        arrays["in_" + name] = a
        io[name] = nc.dram_tensor("in_" + name, a.shape, mybir.dt.from_np(a.dtype), kind="ExternalInput").ap()
    io["out"] = nc.dram_tensor("out", (N, C), F32, kind="ExternalOutput").ap()
    io["xn_d"] = nc.dram_tensor("xn_d", (N, C), F32, kind="Internal").ap()
    io["rec_d"] = nc.dram_tensor("rec_d", (EB * 128, 4), F32, kind="Internal").ap()
    io["xs_d"] = nc.dram_tensor("xs_d", (TB * 128, C), F32, kind="Internal").ap()
    io["ys_d"] = nc.dram_tensor("ys_d", (TB * 128, C), F32, kind="Internal").ap()
    build(nc, io)
    return run_bass_kernel_spmd(nc, [arrays], core_ids=[0]).results[0]["out"]
```
